# Optimizing a Trainium2 kernel written in Bass

```python
import numpy as np
import jax
import jax.numpy as jnp

def _softmax(x, axis=-1):
    return jax.nn.softmax(x, axis=axis)

def _gelu(x):
    return jax.nn.gelu(x, approximate=True)

def _silu(x):
    return jax.nn.silu(x)

def _sigmoid(x):
    return jax.nn.sigmoid(x)

def _layernorm(x, axis=-1, eps=1e-05):
    m = jnp.mean(x, axis=axis, keepdims=True)
    v = jnp.var(x, axis=axis, keepdims=True)
    return (x - m) / jnp.sqrt(v + eps)

def _scatter_add(tgt, idx, src, axis=0):
    return tgt.at[idx].add(src)

def _segment_sum(src, seg, n):
    return jax.ops.segment_sum(src, seg, n)
kernel_name = 'mk_macaron_d2_jaxref_r4_085720'

def setup_inputs(seed: int=0):
    np.random.seed(seed)
    _w = jnp.asarray

    def _L0_attn_setup():
        import jax, jax.numpy as jnp
        import numpy as np
        D_MODEL = 256
        NUM_HEADS = 16
        HEAD_DIM = D_MODEL // NUM_HEADS
        CHUNK = 64
        B, T = (4, 1024)

        def l2norm(x, eps=1e-06):
            return x * jax.lax.rsqrt(jnp.sum(x * x, axis=-1, keepdims=True) + eps)

        def _forward(x, Wq, Wk, Wv, Wg, Wo, Wb, Wa, dt_bias, A_log, norm_w):
            Bb, Tt, D = x.shape
            H, K, C = (NUM_HEADS, HEAD_DIM, CHUNK)
            n = Tt // C
            q = l2norm((x @ Wq).reshape(Bb, Tt, H, K)) / np.sqrt(K)
            k = l2norm((x @ Wk).reshape(Bb, Tt, H, K))
            v = (x @ Wv).reshape(Bb, Tt, H, K)
            gate = (x @ Wg).reshape(Bb, Tt, H, K)
            beta = jax.nn.sigmoid(x @ Wb)
            decay = -jnp.exp(A_log)[None, None, :] * jax.nn.softplus(x @ Wa + dt_bias)
            q = jnp.transpose(q, (0, 2, 1, 3)).astype(jnp.float32)
            k = jnp.transpose(k, (0, 2, 1, 3)).astype(jnp.float32)
            v = jnp.transpose(v, (0, 2, 1, 3)).astype(jnp.float32)
            beta_h = jnp.transpose(beta, (0, 2, 1))[..., None]
            v = v * beta_h
            k_beta = k * beta_h
            q = q.reshape(Bb, H, n, C, K)
            k = k.reshape(Bb, H, n, C, K)
            v = v.reshape(Bb, H, n, C, K)
            k_beta = k_beta.reshape(Bb, H, n, C, K)
            g = jnp.cumsum(jnp.transpose(decay, (0, 2, 1)).reshape(Bb, H, n, C), axis=-1)
            tril = jnp.tril(jnp.ones((C, C), bool))
            strict = jnp.tril(jnp.ones((C, C), bool), -1)
            diff = g[..., :, None] - g[..., None, :]
            L = jnp.where(tril, jnp.exp(jnp.where(tril, diff, 0.0)), 0.0)
            P = jnp.where(strict, jnp.einsum('bhncd,bhnmd->bhncm', k_beta, k) * L, 0.0)
            Ainv = jnp.eye(C, dtype=P.dtype) + P
            Pk = P
            for _ in range(int(np.ceil(np.log2(C))) - 1):
                Pk = Pk @ Pk
                Ainv = Ainv + Pk @ Ainv
            v = Ainv @ v
            k_cumdecay = Ainv @ (k_beta * jnp.exp(g)[..., None])

            def step(S, inp):
                q_i, k_i, v_i, kcd_i, g_i, L_i = inp
                attn = jnp.where(tril, jnp.einsum('bhck,bhmk->bhcm', q_i, k_i) * L_i, 0.0)
                v_new = v_i - kcd_i @ S
                o_i = q_i * jnp.exp(g_i)[..., None] @ S + attn @ v_new
                g_last = g_i[..., -1:]
                S_new = S * jnp.exp(g_last)[..., None] + jnp.einsum('bhck,bhcd->bhkd', k_i * jnp.exp(g_last - g_i)[..., None], v_new)
                return (S_new, o_i)
            to_scan = lambda a: jnp.moveaxis(a, 2, 0)
            S0 = jnp.zeros((Bb, H, K, K), jnp.float32)
            _, o = jax.lax.scan(step, S0, (to_scan(q), to_scan(k), to_scan(v), to_scan(k_cumdecay), to_scan(g), to_scan(L)))
            o = jnp.transpose(o, (1, 0, 3, 2, 4)).reshape(Bb, Tt, H, K)
            o = o * jax.lax.rsqrt(jnp.mean(o * o, axis=-1, keepdims=True) + 1e-05) * norm_w
            o = o * jax.nn.silu(gate)
            return o.reshape(Bb, Tt, D) @ Wo
        key = jax.random.key(seed)
        ks = jax.random.split(key, 10)
        s = 1.0 / np.sqrt(D_MODEL)
        inp = {'x': jax.random.normal(ks[0], (B, T, D_MODEL), jnp.float32), 'Wq': jax.random.normal(ks[1], (D_MODEL, D_MODEL), jnp.float32) * s, 'Wk': jax.random.normal(ks[2], (D_MODEL, D_MODEL), jnp.float32) * s, 'Wv': jax.random.normal(ks[3], (D_MODEL, D_MODEL), jnp.float32) * s, 'Wg': jax.random.normal(ks[4], (D_MODEL, D_MODEL), jnp.float32) * s, 'Wo': jax.random.normal(ks[5], (D_MODEL, D_MODEL), jnp.float32) * s, 'Wb': jax.random.normal(ks[6], (D_MODEL, NUM_HEADS), jnp.float32) * s, 'Wa': jax.random.normal(ks[7], (D_MODEL, NUM_HEADS), jnp.float32) * s, 'dt_bias': jnp.ones((NUM_HEADS,), jnp.float32), 'A_log': jnp.log(jax.random.uniform(ks[8], (NUM_HEADS,), jnp.float32, 0.001, 16.0)), 'norm_w': jnp.ones((HEAD_DIM,), jnp.float32)}
        return inp
    _L0_attn_in = _L0_attn_setup()

    def _L0_ffn_setup():
        import jax, jax.numpy as jnp
        import numpy as np
        DIM = 256
        HIDDEN = 768
        SCALE = 1.0 / 127.0

        def _dequant(w_int, dtype):
            return w_int.astype(dtype) * jnp.asarray(SCALE, dtype)
        key = jax.random.key(seed)
        k_x, k_g, k_u, k_d = jax.random.split(key, 4)
        x = jax.random.normal(k_x, (4, 512, DIM), dtype=jnp.float32)
        w_gate = jax.random.randint(k_g, (HIDDEN, DIM), -127, 128, dtype=jnp.int32)
        w_up = jax.random.randint(k_u, (HIDDEN, DIM), -127, 128, dtype=jnp.int32)
        w_down = jax.random.randint(k_d, (DIM, HIDDEN), -127, 128, dtype=jnp.int32)
        return {'x': x, 'w_gate': w_gate, 'w_up': w_up, 'w_down': w_down}
    _L0_ffn_in = _L0_ffn_setup()

    def _L1_attn_setup():
        import jax, jax.numpy as jnp
        import numpy as np
        B, L, D, N = (2, 2048, 256, 128)
        EPS = 1e-05
        key = jax.random.key(seed)
        ks = jax.random.split(key, 6)
        x = jax.random.normal(ks[0], (B, L, D), dtype=jnp.float32)
        Lambda_real = jax.random.normal(ks[1], (N,), dtype=jnp.float32)
        Lambda_imag = jax.random.normal(ks[2], (N,), dtype=jnp.float32)
        C_real = jax.random.normal(ks[3], (D, N), dtype=jnp.float32)
        C_imag = jax.random.normal(ks[4], (D, N), dtype=jnp.float32)
        param_D = jax.random.normal(ks[5], (D,), dtype=jnp.float32)
        gamma = jnp.ones((D,), dtype=jnp.float32)
        beta = jnp.zeros((D,), dtype=jnp.float32)
        return {'x': x, 'Lambda_real': Lambda_real, 'Lambda_imag': Lambda_imag, 'C_real': C_real, 'C_imag': C_imag, 'param_D': param_D, 'gamma': gamma, 'beta': beta}
    _L1_attn_in = _L1_attn_setup()

    def _L1_ffn_setup():
        import jax, jax.numpy as jnp
        import numpy as np
        MAX_VAL = 100.0
        key = jax.random.key(seed)
        k1, k2, k3 = jax.random.split(key, 3)
        B, S, D_IN, D_OUT = (4, 2048, 256, 256)
        x = jax.random.normal(k1, (B, S, D_IN), dtype=jnp.float32)
        weights = jax.random.normal(k2, (D_OUT, D_IN), dtype=jnp.float32)
        scale = jnp.ones((D_OUT,), dtype=jnp.float32)
        bias = jax.random.normal(k3, (D_OUT,), dtype=jnp.float32)
        return {'x': x, 'weights': weights, 'scale': scale, 'bias': bias}
    _L1_ffn_in = _L1_ffn_setup()
    _d = {'L0_attn_x': _L0_attn_in['x'], 'L0_attn_Wq': _L0_attn_in['Wq'], 'L0_attn_Wk': _L0_attn_in['Wk'], 'L0_attn_Wv': _L0_attn_in['Wv'], 'L0_attn_Wg': _L0_attn_in['Wg'], 'L0_attn_Wo': _L0_attn_in['Wo'], 'L0_attn_Wb': _L0_attn_in['Wb'], 'L0_attn_Wa': _L0_attn_in['Wa'], 'L0_attn_dt_bias': _L0_attn_in['dt_bias'], 'L0_attn_A_log': _L0_attn_in['A_log'], 'L0_attn_norm_w': _L0_attn_in['norm_w'], 'L0_ffn_w_gate': _L0_ffn_in['w_gate'], 'L0_ffn_w_up': _L0_ffn_in['w_up'], 'L0_ffn_w_down': _L0_ffn_in['w_down'], 'L1_attn_Lambda_real': _L1_attn_in['Lambda_real'], 'L1_attn_Lambda_imag': _L1_attn_in['Lambda_imag'], 'L1_attn_C_real': _L1_attn_in['C_real'], 'L1_attn_C_imag': _L1_attn_in['C_imag'], 'L1_attn_param_D': _L1_attn_in['param_D'], 'L1_attn_gamma': _L1_attn_in['gamma'], 'L1_attn_beta': _L1_attn_in['beta'], 'L1_ffn_weights': _L1_ffn_in['weights'], 'L1_ffn_scale': _L1_ffn_in['scale'], 'L1_ffn_bias': _L1_ffn_in['bias']}
    _x0 = _d['L0_attn_x']
    _d['L0_attn_x'] = jax.random.normal(jax.random.fold_in(jax.random.key(seed), 1), (2, 2048, 256), dtype=_x0.dtype)
    del _x0
    return _d

def reference(L0_attn_x, L0_attn_Wq, L0_attn_Wk, L0_attn_Wv, L0_attn_Wg, L0_attn_Wo, L0_attn_Wb, L0_attn_Wa, L0_attn_dt_bias, L0_attn_A_log, L0_attn_norm_w, L0_ffn_w_gate, L0_ffn_w_up, L0_ffn_w_down, L1_attn_Lambda_real, L1_attn_Lambda_imag, L1_attn_C_real, L1_attn_C_imag, L1_attn_param_D, L1_attn_gamma, L1_attn_beta, L1_ffn_weights, L1_ffn_scale, L1_ffn_bias):

    def _L0_attn_ref(x, Wq, Wk, Wv, Wg, Wo, Wb, Wa, dt_bias, A_log, norm_w):
        import jax, jax.numpy as jnp
        import numpy as np
        D_MODEL = 256
        NUM_HEADS = 16
        HEAD_DIM = D_MODEL // NUM_HEADS
        CHUNK = 64
        B, T = (4, 1024)

        def l2norm(x, eps=1e-06):
            return x * jax.lax.rsqrt(jnp.sum(x * x, axis=-1, keepdims=True) + eps)

        def _forward(x, Wq, Wk, Wv, Wg, Wo, Wb, Wa, dt_bias, A_log, norm_w):
            Bb, Tt, D = x.shape
            H, K, C = (NUM_HEADS, HEAD_DIM, CHUNK)
            n = Tt // C
            q = l2norm((x @ Wq).reshape(Bb, Tt, H, K)) / np.sqrt(K)
            k = l2norm((x @ Wk).reshape(Bb, Tt, H, K))
            v = (x @ Wv).reshape(Bb, Tt, H, K)
            gate = (x @ Wg).reshape(Bb, Tt, H, K)
            beta = jax.nn.sigmoid(x @ Wb)
            decay = -jnp.exp(A_log)[None, None, :] * jax.nn.softplus(x @ Wa + dt_bias)
            q = jnp.transpose(q, (0, 2, 1, 3)).astype(jnp.float32)
            k = jnp.transpose(k, (0, 2, 1, 3)).astype(jnp.float32)
            v = jnp.transpose(v, (0, 2, 1, 3)).astype(jnp.float32)
            beta_h = jnp.transpose(beta, (0, 2, 1))[..., None]
            v = v * beta_h
            k_beta = k * beta_h
            q = q.reshape(Bb, H, n, C, K)
            k = k.reshape(Bb, H, n, C, K)
            v = v.reshape(Bb, H, n, C, K)
            k_beta = k_beta.reshape(Bb, H, n, C, K)
            g = jnp.cumsum(jnp.transpose(decay, (0, 2, 1)).reshape(Bb, H, n, C), axis=-1)
            tril = jnp.tril(jnp.ones((C, C), bool))
            strict = jnp.tril(jnp.ones((C, C), bool), -1)
            diff = g[..., :, None] - g[..., None, :]
            L = jnp.where(tril, jnp.exp(jnp.where(tril, diff, 0.0)), 0.0)
            P = jnp.where(strict, jnp.einsum('bhncd,bhnmd->bhncm', k_beta, k) * L, 0.0)
            Ainv = jnp.eye(C, dtype=P.dtype) + P
            Pk = P
            for _ in range(int(np.ceil(np.log2(C))) - 1):
                Pk = Pk @ Pk
                Ainv = Ainv + Pk @ Ainv
            v = Ainv @ v
            k_cumdecay = Ainv @ (k_beta * jnp.exp(g)[..., None])

            def step(S, inp):
                q_i, k_i, v_i, kcd_i, g_i, L_i = inp
                attn = jnp.where(tril, jnp.einsum('bhck,bhmk->bhcm', q_i, k_i) * L_i, 0.0)
                v_new = v_i - kcd_i @ S
                o_i = q_i * jnp.exp(g_i)[..., None] @ S + attn @ v_new
                g_last = g_i[..., -1:]
                S_new = S * jnp.exp(g_last)[..., None] + jnp.einsum('bhck,bhcd->bhkd', k_i * jnp.exp(g_last - g_i)[..., None], v_new)
                return (S_new, o_i)
            to_scan = lambda a: jnp.moveaxis(a, 2, 0)
            S0 = jnp.zeros((Bb, H, K, K), jnp.float32)
            _, o = jax.lax.scan(step, S0, (to_scan(q), to_scan(k), to_scan(v), to_scan(k_cumdecay), to_scan(g), to_scan(L)))
            o = jnp.transpose(o, (1, 0, 3, 2, 4)).reshape(Bb, Tt, H, K)
            o = o * jax.lax.rsqrt(jnp.mean(o * o, axis=-1, keepdims=True) + 1e-05) * norm_w
            o = o * jax.nn.silu(gate)
            return o.reshape(Bb, Tt, D) @ Wo
        return _forward(x, Wq, Wk, Wv, Wg, Wo, Wb, Wa, dt_bias, A_log, norm_w)

    def _L0_ffn_ref(x, w_gate, w_up, w_down):
        import jax, jax.numpy as jnp
        import numpy as np
        DIM = 256
        HIDDEN = 768
        SCALE = 1.0 / 127.0

        def _dequant(w_int, dtype):
            return w_int.astype(dtype) * jnp.asarray(SCALE, dtype)
        wg = _dequant(w_gate, x.dtype)
        wu = _dequant(w_up, x.dtype)
        wd = _dequant(w_down, x.dtype)
        gate = jnp.einsum('bsd,hd->bsh', x, wg)
        up = jnp.einsum('bsd,hd->bsh', x, wu)
        h = jax.nn.silu(gate) * up
        return jnp.einsum('bsh,dh->bsd', h, wd)

    def _L1_attn_ref(x, Lambda_real, Lambda_imag, C_real, C_imag, param_D, gamma, beta):
        import jax, jax.numpy as jnp
        import numpy as np
        B, L, D, N = (2, 2048, 256, 128)
        EPS = 1e-05
        seq_len = x.shape[1]
        mean = jnp.mean(x, axis=-1, keepdims=True)
        var = jnp.mean(jnp.square(x - mean), axis=-1, keepdims=True)
        u = (x - mean) * jax.lax.rsqrt(var + EPS) * gamma + beta
        residual = u * param_D
        Lam = -jnp.exp(Lambda_real) + 1j * jnp.exp(Lambda_imag)
        C = (C_real + 1j * C_imag) * (jnp.exp(Lam) - 1.0) / Lam
        ar = jnp.arange(seq_len, dtype=jnp.float32)
        S = jnp.exp(Lam[:, None] * ar[None, :])
        K = jnp.einsum('hn,nl->lh', C, S).real
        n_fft = seq_len * 2
        u_f = jnp.fft.rfft(u, n=n_fft, axis=-2)
        K_f = jnp.fft.rfft(K, n=n_fft, axis=-2)
        y = jnp.fft.irfft(u_f * K_f, n=n_fft, axis=-2)[..., :seq_len, :]
        return y + residual

    def _L1_ffn_ref(x, weights, scale, bias):
        import jax, jax.numpy as jnp
        import numpy as np
        MAX_VAL = 100.0
        w = (weights >= 0.0).astype(x.dtype) * 2.0 - 1.0
        y = jnp.einsum('bsi,oi->bso', x, w)
        y = y * scale + bias
        y = jnp.clip(y, -MAX_VAL, MAX_VAL)
        return y
    x = L0_attn_x
    x = x + 0.5 * _L0_ffn_ref(_layernorm(x, axis=-1), L0_ffn_w_gate, L0_ffn_w_up, L0_ffn_w_down)
    x = x + _L0_attn_ref(_layernorm(x, axis=-1), L0_attn_Wq, L0_attn_Wk, L0_attn_Wv, L0_attn_Wg, L0_attn_Wo, L0_attn_Wb, L0_attn_Wa, L0_attn_dt_bias, L0_attn_A_log, L0_attn_norm_w)
    x = x + 0.5 * _L0_ffn_ref(_layernorm(x, axis=-1), L0_ffn_w_gate, L0_ffn_w_up, L0_ffn_w_down)
    x = x + 0.5 * _L1_ffn_ref(_layernorm(x, axis=-1), L1_ffn_weights, L1_ffn_scale, L1_ffn_bias)
    x = x + _L1_attn_ref(_layernorm(x, axis=-1), L1_attn_Lambda_real, L1_attn_Lambda_imag, L1_attn_C_real, L1_attn_C_imag, L1_attn_param_D, L1_attn_gamma, L1_attn_beta)
    x = x + 0.5 * _L1_ffn_ref(_layernorm(x, axis=-1), L1_ffn_weights, L1_ffn_scale, L1_ffn_bias)
    return x

_drawn_inputs = setup_inputs


def setup_inputs(seed=0):
    import zlib

    import numpy as np

    out = dict(_drawn_inputs(seed))
    spreads = {'L0_attn_dt_bias': (1.0, 0.2),
     'L0_attn_norm_w': (1.0, 0.2),
     'L1_attn_gamma': (1.0, 0.2),
     'L1_attn_beta': (0.0, 0.1),
     'L1_ffn_scale': (1.0, 0.2)}
    factors = {}
    for name, (base, spread) in spreads.items():
        noise = np.random.default_rng([zlib.crc32(name.encode()), seed]).standard_normal(out[name].shape)
        drawn = base * np.exp(spread * noise) if base else spread * noise
        out[name] = jnp.asarray(drawn.astype(out[name].dtype))
    for name, factor in factors.items():
        out[name] = (out[name] * factor).astype(out[name].dtype)
    return out
```

```python
from contextlib import ExitStack

import concourse.bass as bass
from concourse import mybir

F32 = mybir.dt.float32
F32R = mybir.dt.float32r
I32 = mybir.dt.int32
ALU = mybir.AluOpType
ACT = mybir.ActivationFunctionType
AX_X = mybir.AxisListType.X

P = 128
DM = 256
KD = DM // P
HID = 768
MH = HID // P
NH, HD, CH = 16, 16, 64
G2 = NH * HD // P
BLK = 4
SLOT_LAG = 5
TWO_PI_A = 6.28125
TWO_PI_B = 6.283185307179586 - 6.28125
N_CONST = 6 * P + 8 + 2
RSQRT_GUESS = 1597463007.0
ROUND = 12582912.0


class Engine:

    def __init__(self, name, sem):
        self.name, self.sem, self.count, self.queue, self.seen = name, sem, 0, [], {}

    def wait(self, *tokens):
        for sem, value in [t for t in tokens if t is not None]:
            if self.seen.get(id(sem), 0) < value:
                self.seen[id(sem)] = value
                self.queue.append(lambda eng, s=sem, v=value: eng.wait_ge(s, v))

    def put(self, issue, *tokens, signal=True):
        self.wait(*tokens)
        if not signal:
            self.queue.append(issue)
            return None
        self.count += 1
        self.queue.append(lambda eng, s=self.sem: issue(eng).then_inc(s, 1))
        return (self.sem, self.count)

    def replay(self, eng):
        for step in self.queue:
            step(eng)


def alternate(tasks):
    tasks = list(tasks)
    while tasks:
        for task in list(tasks):
            if next(task, "end") == "end":
                tasks.remove(task)


def build(nc, io, n_tiles, tiles_per_seq):
    NT, TB = n_tiles, tiles_per_seq
    NBLK = NT // BLK
    ctx = ExitStack()
    with ctx:
        def sem(name):
            return ctx.enter_context(nc.semaphore(name))

        def sb(name, cols, dt=F32):
            return ctx.enter_context(nc.sbuf_tensor(name, [P, cols], dt))

        pe, act, dve, pool, sp = (Engine(n, sem(f"{n}_done")) for n in ("pe", "act", "dve", "pool", "sp"))
        bank = [ctx.enter_context(nc.psum_tensor(f"bank{i}", [P, 512], F32)) for i in range(8)]

        X_sb = sb("X", NT * DM)
        X = X_sb[:].rearrange("p (t d) -> p t d", t=NT)
        stats = sb("ln_stats", 6 * BLK)
        mean_var = sb("ln_mean_var", 2 * NT)
        MV = mean_var[:].rearrange("p (t two) -> p t two", two=2)
        rstd = sb("ln_rstd", NT)
        newton = sb("newton", 4 * NT)
        consts = sb("consts", N_CONST)
        ident = consts[:, 0:P]
        upto = consts[:, P:2 * P]
        after = consts[:, 2 * P:3 * P]
        before = consts[:, 3 * P:4 * P]
        head_diag = consts[:, 4 * P:5 * P]
        head_rows = consts[:, 5 * P:5 * P + 8]
        chunk_rows = consts[:, 5 * P + 8:5 * P + 10]
        flip = consts[:, 5 * P + 10:6 * P + 10]
        w_gate = sb("w_gate", KD * HID)
        w_up = sb("w_up", KD * HID)
        w_down = sb("w_down", MH * DM)
        w_bin = sb("w_bin", KD * DM)
        scale_row = sb("scale_row", DM)
        bias_row = sb("bias_row", DM)
        gamma_row = sb("gamma_row", DM)
        beta_row = sb("beta_row", DM)
        pow_re = sb("pow_re", P + 1)
        pow_im = sb("pow_im", P + 1)
        neg_pow_im = sb("neg_pow_im", P + 1)
        into_re = sb("into_re", P)
        into_im = sb("into_im", P)
        C_re = sb("C_re", DM)
        C_im = sb("C_im", DM)
        step_im_neg = sb("step_im_neg", 1)
        lent = [ExitStack()]
        taken = [0]

        def take(cols):
            taken[0] += 1
            return lent[0].enter_context(nc.sbuf_tensor(f"lent{taken[0]}", [P, cols], F32))[:]

        all_engines = (pe, act, dve, pool, sp)
        dma_tokens = []

        def load(name, dst, src, *tokens):
            s = sem(name)
            sp.wait(*tokens)
            sp.queue.append(lambda eng: eng.dma_start(dst, src).then_inc(s, 16))
            dma_tokens.append((s, 16))
            return (s, 16)

        def phase():
            now = [(e.sem, e.count) for e in (pe, act, dve, pool) if e.count] + list(dma_tokens)
            for e in all_engines:
                e.wait(*now)
            lent[0].close()
            lent[0] = ExitStack()

        def copy_act(dst, src, *tok):
            return act.put(lambda e: e.activation(dst, src, ACT.Copy), *tok)

        def copy(dst, src, *tok):
            return dve.put(lambda e: e.tensor_copy(dst, src), *tok)

        def tt(eng, dst, a, b, op, *tok):
            return eng.put(lambda e: e.tensor_tensor(dst, a, b, op), *tok)

        def ts(eng, dst, a, s1, s2, op0, op1, *tok):
            if op1 is None:
                return eng.put(lambda e: e.tensor_scalar(dst, a, s1, None, op0), *tok)
            return eng.put(lambda e: e.tensor_scalar(dst, a, s1, s2, op0, op1), *tok)

        def stt(dst, a, s, b, op0, op1, *tok):
            return dve.put(lambda e: e.scalar_tensor_tensor(out=dst, in0=a, scalar=s, in1=b, op0=op0, op1=op1), *tok)

        def activate(dst, src, func, *tok, scale=1.0):
            return act.put(lambda e: e.activation(dst, src, func, scale=scale), *tok)

        def mm(dst, lhsT, rhs, *tok, start=True, stop=True, signal=True):
            return pe.put(lambda e: e.matmul(dst, lhsT, rhs, start=start, stop=stop), *tok, signal=signal)

        def turn(dst, src, *tok, signal=True):
            return pe.put(lambda e: e.transpose(dst, src, ident), *tok, signal=signal)

        def bcast_last(ap, n):
            a = ap.shape[1]
            return ap.unsqueeze(2).to_broadcast([ap.shape[0], a, n])

        def bcast_mid(ap, n):
            return ap.unsqueeze(1).to_broadcast([ap.shape[0], n, ap.shape[1]])

        def inverse_sqrt(dst, src, times, eps, work, *tok, newton_on=None):
            n = dst.shape[1]
            v, y, t = (work[:, k * n:(k + 1) * n] for k in range(3))
            d = ts(dve, v, src, times, eps, ALU.mult, ALU.add, *tok)
            d = ts(dve, t.bitcast(I32), v.bitcast(I32), 1, None, ALU.logical_shift_right, None, d)
            d = ts(dve, y.bitcast(I32), t.bitcast(I32), -1.0, RSQRT_GUESS, ALU.mult, ALU.add, d)
            for step in range(3):
                to = dst if step == 2 else y
                if newton_on is pool:
                    d = tt(pool, t, y, y, ALU.mult, d)
                    d = tt(pool, t, t, v, ALU.mult, d)
                    d = ts(pool, t, t, -0.5, 1.5, ALU.mult, ALU.add, d)
                    d = tt(pool, to, t, y, ALU.mult, d)
                else:
                    d = tt(dve, t, y, y, ALU.mult, d)
                    d = stt(t, t, -0.5, v, ALU.mult, ALU.mult, d)
                    d = stt(to, t, 1.5, y, ALU.add, ALU.mult, d)
            return d


        def tile_stats(t, *tok):
            s = stats[:, 6 * (t % BLK):6 * (t % BLK) + 6]
            d = dve.put(lambda e: e.bn_stats(s, X[:, t, :]), *tok)
            return dve.put(lambda e: e.bn_aggr(MV[:, t, :], s), d)

        def norm_factors(*tok):
            norm_ready[0] = inverse_sqrt(rstd[:], MV[:, :, 1], 1.0, 1e-5, newton[:], *tok)
            return norm_ready[0]

        norm_ready = [None]

        def normalize(dst, t, *tok):
            return ts(dve, dst, X[:, t, :], MV[:, t, 0:1], rstd[:, t:t + 1], ALU.subtract, ALU.mult, norm_ready[0], *tok)

        def split(hi, lo, src, *tok):
            a = copy_act(hi.bitcast(F32R), src, *tok)
            return a, tt(dve, lo.bitcast(F32R), src, hi, ALU.subtract, a)

        const_in = load("consts_in", consts[:], io["consts"])
        x_in = []
        x_tiles = io["x"].rearrange("(t p) d -> p t d", p=P)
        for b in range(NBLK):
            x_in.append(load(f"x_in{b}", X[:, BLK * b:BLK * b + BLK, :], x_tiles[:, BLK * b:BLK * b + BLK, :]))

        def integer_weights(name, dst, src, rows):
            n = dst.shape[1]
            raw = take(n)
            got = load(name + "_in", raw.bitcast(I32).rearrange("p (k n) -> p k n", k=rows),
                       src.rearrange("(k p) n -> p k n", p=P))
            return pool.put(lambda e: e.tensor_copy(dst.bitcast(F32R), raw.bitcast(I32)), got)

        wg_ready = integer_weights("w_gate", w_gate[:], io["w_gate"], KD)
        wu_ready = integer_weights("w_up", w_up[:], io["w_up"], KD)
        wd_ready = integer_weights("w_down", w_down[:], io["w_down"], MH)
        bin_raw = take(KD * DM)
        got = load("w_bin_in", bin_raw.rearrange("p (k n) -> p k n", k=KD), io["w_bin"].rearrange("(k p) n -> p k n", p=P))
        d = ts(dve, bin_raw, bin_raw, 0.0, 2.0, ALU.is_ge, ALU.mult, got)
        wbin_ready = ts(dve, w_bin[:].bitcast(F32R), bin_raw, -1.0, None, ALU.add, None, d)
        rows_in = [load(f"{n}_in", r[:], bass.AP(tensor=io[n].tensor, offset=0, ap=[[0, P], [1, DM]]))
                   for n, r in (("scale", scale_row), ("bias", bias_row), ("gamma", gamma_row), ("beta", beta_row))]

        lam = take(2)
        Craw = take(2 * DM)
        s_work = take(24)
        col = lambda k: s_work[:, k:k + 1]
        l_in = [load("lam_re_in", lam[:, 0:1], io["lam_re"].rearrange("(n a) -> n a", a=1)),
                load("lam_im_in", lam[:, 1:2], io["lam_im"].rearrange("(n a) -> n a", a=1)),
                load("C_re_in", Craw[:, 0:DM], io["C_re"]), load("C_im_in", Craw[:, DM:], io["C_im"])]
        a = activate(s_work[:, 0:2], lam, ACT.Exp, *l_in)
        a = activate(col(2), col(0), ACT.Exp, a, scale=-1.0)
        d = ts(dve, col(3), col(1), 1.0 / (TWO_PI_A + TWO_PI_B), ROUND, ALU.mult, ALU.add, a)
        d = ts(dve, col(3), col(3), -ROUND, None, ALU.add, None, d)
        d = stt(col(4), col(3), -TWO_PI_A, col(1), ALU.mult, ALU.add, d)
        d = stt(col(4), col(3), -TWO_PI_B, col(4), ALU.mult, ALU.add, d)
        d = ts(dve, col(4), col(4), 3.1415925, -3.1415925, ALU.min, ALU.max, d)
        a = activate(col(5), col(4), ACT.Sin, d)
        a = activate(col(6), col(4), ACT.Sin, d, scale=0.5)
        d = tt(dve, col(7), col(6), col(6), ALU.mult, a)
        d = ts(dve, col(7), col(7), -2.0, 1.0, ALU.mult, ALU.add, d)
        d = dve.put(lambda e: e.memset(pow_re[:, 0:1], 1.0))
        d = dve.put(lambda e: e.memset(pow_im[:, 0:1], 0.0))
        d = tt(dve, pow_re[:, 1:2], col(7), col(2), ALU.mult, d)
        d = tt(dve, pow_im[:, 1:2], col(5), col(2), ALU.mult, a)
        tmp = take(2 * P)
        w = 1
        while w < P:
            R, I = pow_re[:, 1:1 + w], pow_im[:, 1:1 + w]
            br, bi = pow_re[:, w:w + 1], pow_im[:, w:w + 1]
            d = ts(dve, tmp[:, 0:w], I, bi, None, ALU.mult, None, d)
            ts(dve, tmp[:, P:P + w], I, br, None, ALU.mult, None, d)
            d = (dve.sem, dve.count)
            stt(pow_re[:, 1 + w:1 + 2 * w], R, br, tmp[:, 0:w], ALU.mult, ALU.subtract, d)
            d = stt(pow_im[:, 1 + w:1 + 2 * w], R, bi, tmp[:, P:P + w], ALU.mult, ALU.add, d)
            w *= 2
        pow_ready = d
        d = ts(dve, neg_pow_im[:], pow_im[:], -1.0, None, ALU.mult, None, d)
        d = ts(dve, step_im_neg[:], pow_im[:, P:P + 1], -1.0, None, ALU.mult, None, d)
        d = ts(dve, col(8), pow_re[:, 1:2], -1.0, None, ALU.add, None, d)
        d = tt(dve, col(9), col(0), col(0), ALU.mult, d)
        d = tt(dve, col(10), col(1), col(1), ALU.mult, d)
        d = tt(dve, col(9), col(9), col(10), ALU.add, d)
        d = dve.put(lambda e: e.reciprocal(col(9), col(9)), d)
        d = tt(dve, col(11), pow_im[:, 1:2], col(1), ALU.mult, d)
        d = tt(dve, col(12), col(8), col(0), ALU.mult, d)
        d = tt(dve, col(13), col(11), col(12), ALU.subtract, d)
        d = tt(dve, col(13), col(13), col(9), ALU.mult, d)
        d = tt(dve, col(11), pow_im[:, 1:2], col(0), ALU.mult, d)
        d = tt(dve, col(12), col(8), col(1), ALU.mult, d)
        d = tt(dve, col(14), col(11), col(12), ALU.add, d)
        d = tt(dve, col(14), col(14), col(9), ALU.mult, d)
        d = ts(dve, col(14), col(14), -1.0, None, ALU.mult, None, d)
        ctmp = take(2 * DM)
        d = ts(dve, ctmp[:, 0:DM], Craw[:, DM:], col(14), None, ALU.mult, None, d)
        d = ts(dve, ctmp[:, DM:], Craw[:, DM:], col(13), None, ALU.mult, None, d)
        d = stt(C_re[:], Craw[:, 0:DM], col(13), ctmp[:, 0:DM], ALU.mult, ALU.subtract, d)
        c_ready = stt(C_im[:], Craw[:, 0:DM], col(14), ctmp[:, DM:], ALU.mult, ALU.add, d)
        turn(bank[0][:, 0:P], pow_re[:, 0:P], pow_ready, const_in)
        p = turn(bank[0][:, P:2 * P], pow_im[:, 0:P])
        copy_act(into_re[:], bank[0][:, 0:P], p)
        copy_act(into_im[:], bank[0][:, P:2 * P], p)
        taps = take(KD * 2 * P).rearrange("p (k n) -> p k n", k=KD)
        skip_in = load("D_in", s_work[:, 16:18], io["param_D"])
        z = dve.put(lambda e: e.memset(taps, 0.0))
        for k in range(KD):
            o = bank[1 + k][:, 0:P]
            mm(o, C_re[:, k * P:(k + 1) * P], pow_re[:, 0:P], c_ready, stop=False, signal=False)
            p = mm(o, C_im[:, k * P:(k + 1) * P], neg_pow_im[:, 0:P], start=False)
            d = copy(taps[:, k, P:2 * P], o, p, z)
            d = tt(dve, taps[:, k, P:P + 1], taps[:, k, P:P + 1], s_work[:, 16 + k:17 + k], ALU.add, d, skip_in)
        taps_dram = nc.dram_tensor("taps_scratch", (DM, 2 * P), F32, kind="Internal")
        taps_out = load("taps_out", taps_dram.ap().rearrange("(k p) n -> p k n", p=P), taps, d)

        for t in range(NT):
            st = tile_stats(t, x_in[t // BLK])
        phase()

        def transposed_block(b, xn, xn_free, tbanks, tbank_free):
            for j in range(BLK):
                d = normalize(xn[:, j * DM:(j + 1) * DM], BLK * b + j, xn_free if j == 0 else None)
            for k in range(KD):
                for j in range(BLK):
                    p = turn(tbanks[k][:, j * P:(j + 1) * P], xn[:, j * DM + k * P:j * DM + (k + 1) * P],
                             d, tbank_free[k] if j == 0 else None, signal=(j == BLK - 1))
            return p

        def swiglu_ffn():
            inv = 1.0 / 127.0
            norm_factors(st_last[0])
            xn = take(BLK * DM)
            XT = [[[take(512) for _ in range(KD)] for _ in range(2)] for _ in range(2)]
            H = [[take(MH * 512) for _ in range(2)] for _ in range(2)]
            S = [take(512) for _ in range(3)]
            Hf = [take(512) for _ in range(3)]
            gate_bank, up_bank = bank[0:2], bank[2:4]
            tbank, out_bank = bank[4:6], bank[6:8]
            free = {"xn": None, "t": [None, None], "XT": [None, None], "H": [None, None], "g": [None] * 2,
                    "u": [None] * 2, "S": [None] * 3, "Hf": [None] * 3, "o": [None] * 2}
            ready, h_ready = {}, {}
            count = [0, 0]

            def prepare(b):
                s = b % 2
                p = transposed_block(b, xn, free["xn"], tbank, free["t"])
                free["xn"] = p
                for k in range(KD):
                    _, lo = split(XT[s][0][k], XT[s][1][k], tbank[k][:], p, free["XT"][s])
                    free["t"][k] = lo
                ready[b] = lo

            def gate_up(b, m):
                s, r, q = b % 2, count[0] % 2, count[0] % 3
                count[0] += 1
                for w, bk, fr in ((w_gate, gate_bank[r], free["g"][r]), (w_up, up_bank[r], free["u"][r])):
                    for k in range(KD):
                        for hl in range(2):
                            lhs = w[:, k * HID + m * P:k * HID + (m + 1) * P].bitcast(F32R)
                            p = mm(bk[:], lhs, XT[s][hl][k].bitcast(F32R), ready[b], fr,
                                   start=(k == 0 and hl == 0), stop=(k == 1 and hl == 1), signal=(k == 1 and hl == 1))
                    if w is w_gate:
                        a = activate(S[q], bk[:], ACT.Silu, p, free["S"][q], scale=inv)
                        free["g"][r] = a
                if m == MH - 1:
                    free["XT"][s] = p
                d = tt(dve, Hf[q], S[q], up_bank[r][:], ALU.mult, a, p, free["Hf"][q])
                free["u"][r] = free["S"][q] = d
                hi, lo = H[s][0][:, m * 512:(m + 1) * 512], H[s][1][:, m * 512:(m + 1) * 512]
                d = copy(hi.bitcast(F32R), Hf[q], d, free["H"][s])
                g = tt(pool, lo.bitcast(F32R), Hf[q], hi, ALU.subtract, d, free["H"][s])
                free["Hf"][q] = g
                h_ready[b] = g

            def down(b):
                s = b % 2
                for j in range(BLK):
                    t, r = BLK * b + j, count[1] % 2
                    count[1] += 1
                    o = out_bank[r][:, 0:DM]
                    for m in range(MH):
                        for hl in range(2):
                            p = mm(o, H[s][hl][:, m * 512 + j * P:m * 512 + (j + 1) * P].bitcast(F32R),
                                   w_down[:, m * DM:(m + 1) * DM].bitcast(F32R), h_ready[b], free["o"][r],
                                   start=(m == 0 and hl == 0), stop=(m == MH - 1 and hl == 1),
                                   signal=(m == MH - 1 and hl == 1))
                    d = stt(X[:, t, :], o, 0.5 * inv * inv, X[:, t, :], ALU.mult, ALU.add, p)
                    free["o"][r] = d
                    st_last[0] = tile_stats(t, d)
                free["H"][s] = p

            prepare(0)
            for b in range(NBLK):
                for m in range(MH):
                    gate_up(b, m)
                    if m == 1 and b > 0:
                        down(b - 1)
                    if m == 3 and b + 1 < NBLK:
                        prepare(b + 1)
            down(NBLK - 1)
            phase()

        def binary_ffn(last=False):
            norm_factors(st_last[0])
            xn = take(BLK * DM)
            XT = [[[take(512) for _ in range(KD)] for _ in range(2)] for _ in range(2)]
            Y = [take(DM) for _ in range(3)]
            tbank, out_bank = bank[4:6], bank[0:4]
            free = {"xn": None, "t": [None, None], "XT": [None, None], "o": [None] * 4, "Y": [None] * 3}
            ready = {}
            n = [0]

            def prepare(b):
                s = b % 2
                p = transposed_block(b, xn, free["xn"], tbank, free["t"])
                free["xn"] = p
                for k in range(KD):
                    _, lo = split(XT[s][0][k], XT[s][1][k], tbank[k][:], p, free["XT"][s])
                    free["t"][k] = lo
                ready[b] = lo

            def project(b):
                s = b % 2
                for j in range(BLK):
                    t, r, y = BLK * b + j, n[0] % 4, n[0] % 3
                    n[0] += 1
                    o = out_bank[r][:, 0:DM]
                    for k in range(KD):
                        for hl in range(2):
                            p = mm(o, XT[s][hl][k][:, j * P:(j + 1) * P].bitcast(F32R),
                                   w_bin[:, k * DM:(k + 1) * DM].bitcast(F32R), ready[b], free["o"][r],
                                   start=(k == 0 and hl == 0), stop=(k == 1 and hl == 1), signal=(k == 1 and hl == 1))
                    free["XT"][s] = p
                    d = tt(dve, Y[y], o, scale_row[:], ALU.mult, p, free["Y"][y])
                    free["o"][r] = d
                    g = tt(pool, Y[y], Y[y], bias_row[:], ALU.add, d)
                    g = ts(pool, Y[y], Y[y], -100.0, 100.0, ALU.max, ALU.min, g)
                    d = stt(X[:, t, :], Y[y], 0.5, X[:, t, :], ALU.mult, ALU.add, g)
                    free["Y"][y] = d
                    if not last:
                        st_last[0] = tile_stats(t, d)
                if last:
                    load(f"out{b}", io["out"].rearrange("(t p) d -> p t d", p=P)[:, BLK * b:BLK * b + BLK, :],
                         X[:, BLK * b:BLK * b + BLK, :], d)

            prepare(0)
            for b in range(NBLK):
                if b + 1 < NBLK:
                    prepare(b + 1)
                project(b)
            phase()

        def delta_attention():
            QKVG = 4 * DM
            w_in = take(KD * (QKVG + 2 * NH)).rearrange("p (k n) -> p k n", k=KD)
            w_out = take(KD * DM).rearrange("p (k n) -> p k n", k=KD)
            vec = take(2 * NH + DM)
            dt_row, A_row, nw_row = vec[:, 0:NH], vec[:, NH:2 * NH], vec[:, 2 * NH:]
            w_ready = [load(f"{n}_in", w_in[:, :, o:o + c], io[n].rearrange("(k p) n -> p k n", p=P))
                       for n, o, c in (("Wq", 0, DM), ("Wk", DM, DM), ("Wv", 2 * DM, DM), ("Wg", 3 * DM, DM),
                                       ("Wb", QKVG, NH), ("Wa", QKVG + NH, NH))]
            wo_ready = load("Wo_in", w_out, io["Wo"].rearrange("(k p) n -> p k n", p=P))
            v_ready = [load("dt_in", dt_row, bass.AP(tensor=io["dt_bias"].tensor, offset=0, ap=[[0, P], [1, NH]])),
                       load("A_in", A_row, bass.AP(tensor=io["A_log"].tensor, offset=0, ap=[[0, P], [1, NH]])),
                       load("nw_in", nw_row.rearrange("p (h d) -> p h d", h=NH),
                            bass.AP(tensor=io["norm_w"].tensor, offset=0, ap=[[0, P], [0, NH], [1, HD]]))]
            NG = NT * NH
            beta, adec, eg, ekd, ekd2 = (take(NG) for _ in range(5))
            egl = take(G2 * NT * 2)
            mark, lent[0] = lent[0], ExitStack()
            xn = take(BLK * DM)
            XT = [take(512) for _ in range(KD)]
            free_xn, free_t = None, [None, None]
            norm_factors(st_last[0])
            for b in range(NBLK):
                p = transposed_block(b, xn, free_xn, bank[0:2], free_t)
                free_xn = p
                free_t = [copy_act(XT[k], bank[k][:], p) for k in range(KD)]
                for j in range(BLK):
                    t = BLK * b + j
                    o = bank[4 + t // 16][:, (t % 16) * 32:(t % 16) * 32 + 32]
                    for k in range(KD):
                        p = mm(o, XT[k][:, j * P:(j + 1) * P], w_in[:, k, QKVG:], free_t[k], *w_ready,
                               start=(k == 0), stop=(k == KD - 1), signal=(k == KD - 1))
            gates_done = p
            wk = take(3 * NG)
            w0, w1, w2 = (wk[:, i * NG:(i + 1) * NG] for i in range(3))
            for hf in range((NT + 15) // 16):
                nt = min(16, NT - 16 * hf)
                src = bank[4 + hf][:, 0:nt * 32].rearrange("p (t n) -> p t n", n=32)
                dst = slice(hf * 256, hf * 256 + nt * NH)
                a = activate(w0[:, dst].rearrange("p (t n) -> p t n", n=NH), src[:, :, 0:NH], ACT.Exp, gates_done, scale=-1.0)
                d = tt(dve, w1[:, dst].rearrange("p (t n) -> p t n", n=NH), src[:, :, NH:], bcast_mid(dt_row, nt),
                       ALU.add, gates_done, *v_ready, a)
            d = ts(dve, w0, w0, 1.0, None, ALU.add, None, d, a)
            d = dve.put(lambda e: e.reciprocal(beta, w0), d)
            d = ts(dve, w2, w1, -1.0, None, ALU.mult, None, d)
            d = tt(dve, w2, w1, w2, ALU.max, d)
            a = activate(w2, w2, ACT.Exp, d, scale=-1.0)
            d = ts(dve, w2, w2, 1.0, None, ALU.add, None, a)
            a = activate(w2, w2, ACT.Ln, d)
            a2 = activate(A_row, A_row, ACT.Exp, *v_ready)
            d = stt(w2, w1, 0.0, w2, ALU.max, ALU.add, a)
            d = ts(dve, w2, w2, -1.0, None, ALU.mult, None, d)
            d = tt(dve, adec.rearrange("p (t n) -> p t n", n=NH), w2.rearrange("p (t n) -> p t n", n=NH),
                   bcast_mid(A_row, NT), ALU.mult, d, a2)
            dve.put(lambda e: e.tensor_scalar(nw_row, nw_row, 0.5, None, ALU.mult), *v_ready)
            p = mm(bank[0][:, 0:NG], upto, adec, d, *free_t)
            a = activate(eg, bank[0][:, 0:NG], ACT.Exp, p)
            p = mm(bank[1][:, 0:NG], after, adec)
            a = activate(ekd, bank[1][:, 0:NG], ACT.Exp, p)
            d = ts(dve, ekd2, ekd, chunk_rows[:, 1:2], None, ALU.mult, None, a)
            ts(dve, ekd, ekd, chunk_rows[:, 0:1], None, ALU.mult, None, d)
            spread = [take(P), take(P)]
            sfree = [None, None]
            for t in range(NT):
                for g in range(G2):
                    i = t * G2 + g
                    d = copy(spread[i % 2].rearrange("p (h d) -> p h d", h=8),
                             bcast_last(adec[:, t * NH + 8 * g:t * NH + 8 * g + 8], HD), d, sfree[i % 2])
                    p = mm(bank[2][:, 2 * i:2 * i + 2], spread[i % 2], chunk_rows, d)
                    sfree[i % 2] = p
            a = activate(egl, bank[2][:, 0:G2 * NT * 2], ACT.Exp, p)
            phase()
            lent[0] = mark

            def two(cols):
                return [take(cols) for _ in range(2)]

            sq = take(512)
            ssq, rs_qk, nw_work = take(32), two(32), take(96)
            Kn, Qn, Kb = two(DM), two(DM), take(DM)
            FT = two(3 * DM)
            PY0 = two(NH * 160)
            Kd = two(2 * DM)
            Qg, gate_f = two(DM), two(DM)
            UW = two(2 * DM)
            Oin, Qeff = two(DM), two(DM)
            DU, KX, QX, Em, Es = (take(512) for _ in range(5))
            Q0 = two(512)
            AT = [two(512), two(512)]
            Qm = [[take(512) for _ in range(2)] for _ in range(2)]
            PY = [[take(4 * 160) for _ in range(2)] for _ in range(2)]
            QT2 = take(G2 * 2 * P).rearrange("p (g c n) -> p g c n", g=G2, c=2)
            MT = take(512)
            St = [[take(P) for _ in range(2)] for _ in range(G2)]
            o_sb, o_sq, o_ss, o_rs, o_work = take(DM), take(DM), take(NH), take(NH), take(3 * NH)
            oT = take(DM)

            z0 = pool.put(lambda e: e.memset(QT2, 0.0))
            misc_free = [None, None]
            misc_n, misc_held = [0], set()

            def misc():
                while True:
                    for i in (misc_n[0] % 2, (misc_n[0] + 1) % 2):
                        if i not in misc_held:
                            misc_n[0] = i + 1
                            misc_held.add(i)
                            return 6 + i, misc_free[i]
                    yield

            def release(i, tok):
                misc_held.discard(i - 6)
                misc_free[i - 6] = tok

            tile_ready, group_ready = {}, {}
            tile_read = {}

            def hs(ap):
                return ap.rearrange("p (h d) -> p h d", d=HD)

            def prepare(t):
                s = t % 2
                old = tile_read.get(t - 2, ())
                gcol = slice(t * NH, (t + 1) * NH)
                d = normalize(xn_t, t, xn_free[0])
                bi, fr = yield from misc()
                for k in range(KD):
                    p = turn(bank[bi][:, k * P:(k + 1) * P], xn_t[:, k * P:(k + 1) * P], d, fr, signal=(k == KD - 1))
                xn_free[0] = p
                xt_ready = copy_act(xT_t, bank[bi][:, 0:DM], p, xT_free[0])
                release(bi, xt_ready)
                yield
                bi, fr = yield from misc()
                for k in range(KD):
                    p = mm(bank[bi][:], xT_t[:, k * P:(k + 1) * P], w_in[:, k, 0:512], fr, xt_ready,
                           start=(k == 0), stop=(k == 1), signal=(k == 1))
                qk = bank[bi][:].rearrange("p (n d) -> p n d", d=HD)
                a = activate(sq, bank[bi][:], ACT.Square, p, sq_free[0])
                d = dve.put(lambda e: e.tensor_reduce(ssq, sq.rearrange("p (n d) -> p n d", d=HD), AX_X, ALU.add), a)
                sq_free[0] = d
                yield
                d = inverse_sqrt(rs_qk[s], ssq, 1.0, 1e-6, nw_work, d, *old, newton_on=pool)
                d = ts(pool, rs_qk[s][:, 0:NH], rs_qk[s][:, 0:NH], HD ** -0.5, None, ALU.mult, None, d)
                yield
                yield
                dq = tt(dve, hs(Qn[s]), qk[:, 0:NH, :], bcast_last(rs_qk[s][:, 0:NH], HD), ALU.mult, d, *old)
                dk = tt(dve, hs(Kn[s]), qk[:, NH:, :], bcast_last(rs_qk[s][:, NH:], HD), ALU.mult, d, *old)
                release(bi, dk)
                bj, fr = yield from misc()
                for k in range(KD):
                    p2 = mm(bank[bj][:], xT_t[:, k * P:(k + 1) * P], w_in[:, k, 512:1024], fr,
                            start=(k == 0), stop=(k == 1), signal=(k == 1))
                xT_free[0] = p2
                py = PY0[s].rearrange("p (h n) -> p h n", n=160)
                dv = tt(dve, py[:, :, P:P + HD], hs(bank[bj][:, 0:DM]), bcast_last(beta[:, gcol], HD), ALU.mult, p2, *old)
                yield
                g = tt(pool, hs(Kb), hs(Kn[s]), bcast_last(beta[:, gcol], HD), ALU.mult, dk, kb_free[0])
                g2 = tt(pool, py[:, :, P + HD:], hs(Kb), bcast_last(eg[:, gcol], HD), ALU.mult, g, *old)
                a = activate(gate_f[s], bank[bj][:, DM:], ACT.Tanh, p2, dv, *old, scale=0.5)
                d = stt(gate_f[s], gate_f[s], 1.0, bank[bj][:, DM:], ALU.add, ALU.mult, a)
                release(bj, d)
                gw = tt(pool, gate_f[s], gate_f[s], nw_row, ALU.mult, d)
                yield
                gq = tt(pool, hs(Qg[s]), hs(Qn[s]), bcast_last(eg[:, gcol], HD), ALU.mult, dq, *old)
                kd = tt(pool, hs(Kd[s][:, 0:DM]), hs(Kn[s]), bcast_last(ekd[:, gcol], HD), ALU.mult, dk, *old)
                kd = tt(pool, hs(Kd[s][:, DM:]), hs(Kn[s]), bcast_last(ekd2[:, gcol], HD), ALU.mult, dk, *old)
                yield
                bi, fr = yield from misc()
                for i, src in enumerate((Kn[s], Kb)):
                    for k in range(G2):
                        p = turn(bank[bi][:, (2 * i + k) * P:(2 * i + k + 1) * P], src[:, k * P:(k + 1) * P], fr, dk, g,
                                 signal=(i == 1 and k == 1))
                kb_free[0] = p
                a = copy_act(FT[s][:, 0:512], bank[bi][:], p, *old)
                release(bi, a)
                yield
                bi, fr = yield from misc()
                for k in range(G2):
                    p = turn(bank[bi][:, k * P:(k + 1) * P], Qn[s][:, k * P:(k + 1) * P], fr, dq, signal=(k == 1))
                a = copy_act(FT[s][:, 512:768], bank[bi][:, 0:DM], p, *old)
                release(bi, a)
                tile_ready[t] = (a, g2, gw, gq, kd, dv)
                yield

            sq_free, kb_free, xn_free, xT_free = [None], [None], [None], [None]
            xn_t, xT_t = take(DM), take(DM)
            slot_free = [None, None]
            work_free = {"DU": None, "KX": None, "QX": None, "E": None}
            front_ready, q0_read = {}, {}
            at_free = {}
            v4 = lambda ap: ap.rearrange("p (h n) -> p h n", h=4)

            def forms():
                groups = [(t, grp) for t in range(NT) for grp in range(4)]
                todo = {}

                def decays(t, grp):
                    hcol = slice(t * NH + 4 * grp, t * NH + 4 * grp + 4)
                    todo["DU"] = tt(pool, v4(DU), bcast_mid(upto, 4), bcast_last(adec[:, hcol], P), ALU.mult, work_free["DU"])

                decays(*groups[0])
                for n, (t, grp) in enumerate(groups):
                    s, g, slot = t % 2, grp // 2, grp % 2
                    turn_no = 2 * t + grp // 2
                    while t not in tile_ready:
                        yield
                    ready, old = tile_ready[t], tile_read.get(t - 2, ())
                    rows = head_rows[:, 4 * (grp % 2):4 * (grp % 2) + 4]
                    KT, KbT, QT = (FT[s][:, i * DM + g * P:i * DM + (g + 1) * P] for i in range(3))
                    at = AT[slot][turn_no % 2]
                    bi, fr = yield from misc()
                    pd = mm(bank[bi][:], after, DU, todo["DU"], fr)
                    work_free["DU"] = pd
                    a = activate(Em, bank[bi][:], ACT.Exp, pd, work_free["E"])
                    release(bi, a)
                    gk = tt(pool, v4(KX), bcast_mid(KbT, 4), bcast_last(rows, P), ALU.mult, work_free["KX"], *ready)
                    dq = tt(dve, v4(QX), bcast_mid(QT, 4), bcast_last(rows, P), ALU.mult, work_free["QX"], *ready)
                    ge = tt(pool, v4(Es), v4(Em), bcast_mid(before, 4), ALU.mult, a, work_free["E"])
                    gm = tt(pool, v4(Em), v4(Em), bcast_mid(upto, 4), ALU.mult, ge)
                    yield
                    yield
                    while turn_no > 0 and (slot, turn_no - 1) not in q0_read:
                        yield
                    bi, fr = yield from misc()
                    pk = mm(bank[bi][:], KT, KX, gk, fr)
                    work_free["KX"] = pk
                    d = tt(dve, Q0[slot], bank[bi][:], Es, ALU.mult, pk, ge, q0_read.get((slot, turn_no - 1)))
                    release(bi, d)
                    bj, fr = yield from misc()
                    pq = mm(bank[bj][:], KT, QX, dq, fr)
                    work_free["QX"] = pq
                    da = tt(dve, at, bank[bj][:], Em, ALU.mult, pq, gm, at_free.get((slot, turn_no - 2)))
                    release(bj, da)
                    work_free["E"] = da
                    if n + 1 < len(groups):
                        decays(*groups[n + 1])
                    yield
                    bi, fr = yield from misc()
                    for h in range(4):
                        p = turn(bank[bi][:, h * P:(h + 1) * P], Q0[slot][:, h * P:(h + 1) * P], d, fr, signal=(h == 3))
                    py = PY0[s][:, grp * 640:(grp + 1) * 640].rearrange("p (h n) -> p h n", n=160)
                    dp = copy_act(py[:, :, 0:P], v4(bank[bi][:]), p, *old)
                    release(bi, dp)
                    front_ready[(t, grp)] = (d, da, dp, ready[-1], ready[1])
                    yield

            def solve(t, grp, slot):
                s, g = t % 2, grp // 2
                turn_no = 2 * t + grp // 2
                bq, b0, b1 = bank[3 * slot], bank[3 * slot + 1], bank[3 * slot + 2]
                while (t, grp) not in front_ready:
                    yield
                dqr, da, dp, *rhs_ready = front_ready[(t, grp)]
                pe.wait(slot_free[slot], *rhs_ready)
                dve.wait(*rhs_ready)
                dy = da
                at = AT[slot][turn_no % 2]
                Q = Q0[slot]
                py = PY0[s][:, grp * 640:(grp + 1) * 640].rearrange("p (h n) -> p h n", n=160)
                for lev in range(3):
                    Qn_, PYn = Qm[slot][(lev + 1) % 2], PY[slot][lev % 2].rearrange("p (h n) -> p h n", n=160)
                    for h in range(4):
                        bk = (b0, b1)[h // 2]
                        p1 = mm(bk[:, (h % 2) * 160:(h % 2) * 160 + 160], Q[:, h * P:(h + 1) * P], py[:, h, :],
                                dp, dqr, dy, signal=(h == 3))
                    for h in range(4):
                        p2 = mm(bq[:, h * P:(h + 1) * P], py[:, h, 0:P], Q[:, h * P:(h + 1) * P], signal=(h == 3))
                    for i, bk in enumerate((b0, b1)):
                        src = bk[:, 0:320].rearrange("p (h n) -> p h n", n=160)
                        dp = copy_act(PYn[:, 2 * i:2 * i + 2, 0:P], src[:, :, 0:P], p1)
                        dy = tt(dve, PYn[:, 2 * i:2 * i + 2, P:], src[:, :, P:], py[:, 2 * i:2 * i + 2, P:], ALU.add, p1, dp)
                    dqr = copy(Qn_, bq[:], p2)
                    if lev == 0:
                        q0_read[(slot, turn_no)] = p2
                    Q, py = Qn_, PYn
                    yield
                last = PY[slot][1].rearrange("p (h n) -> p h n", n=160)
                for h in range(4):
                    p1 = mm(b0[:, h * 32:h * 32 + 32], Q[:, h * P:(h + 1) * P], py[:, h, P:], dy, dqr, signal=(h == 3))
                for h in range(4):
                    p2 = mm(bq[:, h * P:(h + 1) * P], py[:, h, 0:P], Q[:, h * P:(h + 1) * P], dp, signal=(h == 3))
                ps0 = b0[:, 0:P].rearrange("p (h n) -> p h n", n=32)
                dy = tt(dve, last[:, :, P:], ps0, py[:, :, P:], ALU.add, p1)
                Qn_ = Qm[slot][0]
                dqr = copy(Qn_, bq[:], p2)
                Q = Qn_
                yield
                for h in range(4):
                    p1 = mm(b1[:, h * 32:h * 32 + 32], Q[:, h * P:(h + 1) * P], last[:, h, P:], dy, dqr, signal=(h == 3))
                ps1 = b1[:, 0:P].rearrange("p (h n) -> p h n", n=32)
                Y5 = PY[slot][0].rearrange("p (h n) -> p h n", n=160)
                dy = tt(dve, Y5[:, :, P:], ps1, last[:, :, P:], ALU.add, p1)
                yield
                for h in range(4):
                    p1 = mm(b0[:, h * 32:h * 32 + 32], Q[:, h * P:(h + 1) * P], Y5[:, h, P:], dy, signal=(h == 3))
                dz = copy(last[:, :, P:], ps0, p1)
                yield
                for h in range(4):
                    p1 = mm(b1[:, h * 32:h * 32 + 32], Q[:, h * P:(h + 1) * P], last[:, h, P:], dz, signal=(h == 3))
                uw = UW[s].rearrange("p (w h d) -> p h w d", w=2, h=NH)[:, 4 * grp:4 * grp + 4]
                dy = tt(dve, uw, b1[:, 0:P].rearrange("p (h w d) -> p h w d", w=2, d=HD),
                        Y5[:, :, P:].rearrange("p h (w d) -> p h w d", w=2), ALU.add, p1, *tile_read.get(t - 2, ()))
                dy2 = tt(dve, Y5[:, :, 0:32], ps1, Y5[:, :, P:], ALU.add, p1)
                yield
                for h in range(4):
                    p1 = mm(b0[:, h * 32:h * 32 + 32], at[:, h * P:(h + 1) * P], Y5[:, h, 0:32], dy2, da, signal=(h == 3))
                at_free[(slot, turn_no)] = p1
                hsl = slice(grp * 64, grp * 64 + 64)
                old = tile_read.get(t - 2, ())
                d1 = dve.put(lambda e: e.tensor_copy(hs(Oin[s][:, hsl]), ps0[:, :, 0:HD]), p1, *old)
                d2 = tt(dve, hs(Qeff[s][:, hsl]), hs(Qg[s][:, hsl]), ps0[:, :, HD:], ALU.subtract, p1, *old)
                slot_free[slot] = d2
                group_ready[(t, grp)] = d2
                yield

            s_tok = [None] * G2
            qt_free, mt_free, o_free, oT_free = [z0] * G2, [None], [None], [None]

            def scan(t):
                s = t % 2
                done = [group_ready[(t, g)] for g in range(4)]
                seq_start = t % TB == 0
                U, W = UW[s][:, 0:DM], UW[s][:, DM:]
                bi, fr = yield from misc()
                for g in range(G2):
                    p = turn(bank[bi][:, g * P:(g + 1) * P], Qeff[s][:, g * P:(g + 1) * P], fr, *done, signal=(g == G2 - 1))
                for c in range(2):
                    v = bank[bi][:, 0:DM].rearrange("p (g n) -> p g n", g=G2)
                    a = copy_act(QT2[:, :, c, c * CH:(c + 1) * CH], v[:, :, c * CH:(c + 1) * CH], p, *qt_free)
                release(bi, a)
                yield
                bi, fr = yield from misc()
                kd2 = Kd[s].rearrange("p (c n) -> p c n", c=2)
                for g in range(G2):
                    p = mm(bank[bi][:, g * DM:(g + 1) * DM], W[:, g * P:(g + 1) * P], kd2[:, :, g * P:(g + 1) * P],
                           fr, *done, *tile_ready[t], signal=(g == G2 - 1))
                d = tt(dve, MT.rearrange("p (n m) -> p n m", n=4), bank[bi][:].rearrange("p (n m) -> p n m", n=4),
                       bcast_mid(head_diag, 4), ALU.mult, p, mt_free[0])
                release(bi, d)
                for i in range(4):
                    c = (t * G2 + i // 2) * 2 + i % 2
                    dm = stt(MT[:, i * P:(i + 1) * P], ident, egl[:, c:c + 1], MT[:, i * P:(i + 1) * P],
                             ALU.mult, ALU.subtract, d)
                yield
                if seq_start:
                    for g in range(G2):
                        s_tok[g] = dve.put(lambda e, g=g: e.memset(St[g][0], 0.0), s_free[g])
                bu, fru = yield from misc()
                for c in range(2):
                    for g in range(G2):
                        cur = St[g][c]
                        u = bank[bu][:, (2 * g + c) * P:(2 * g + c + 1) * P]
                        mm(u, Kd[s][:, c * DM + g * P:c * DM + (g + 1) * P], U[:, g * P:(g + 1) * P], fru, dm,
                           *s_tok, stop=False, signal=False)
                        p = mm(u, MT[:, (2 * g + c) * P:(2 * g + c + 1) * P], cur, start=False)
                        s_hold[(g, c)] = s_tok[g]
                    for g in range(G2):
                        u = bank[bu][:, (2 * g + c) * P:(2 * g + c + 1) * P]
                        s_tok[g] = tt(dve, St[g][1] if c == 0 else S_end[g], u, head_diag, ALU.mult, p, s_free[g],
                                      s_end_free[g])
                    yield
                release(bu, s_tok[G2 - 1])
                bo, fro = yield from misc()
                for g in range(G2):
                    o = bank[bo][:, g * P:(g + 1) * P]
                    mm(o, QT2[:, g, 0, :], St[g][0], fro, a, s_hold[(g, 0)], stop=False, signal=False)
                    p = mm(o, QT2[:, g, 1, :], St[g][1], s_hold[(g, 1)], start=False)
                    qt_free[g] = p
                    s_free[g] = p
                mt_free[0] = p
                for g in range(G2):
                    s_tok[g] = pool.put(lambda e, g=g: e.tensor_copy(St[g][0], S_end[g]), s_tok[g], p)
                    s_end_free[g] = s_tok[g]
                yield
                d = tt(dve, o_sb, bank[bo][:, 0:DM], Oin[s], ALU.add, p, o_free[0])
                release(bo, d)
                g_ = tt(pool, o_sq, o_sb, o_sb, ALU.mult, d)
                dr = dve.put(lambda e: e.tensor_reduce(o_ss, hs(o_sq), AX_X, ALU.add), g_)
                dr = inverse_sqrt(o_rs, o_ss, 1.0 / HD, 1e-5, o_work, dr, newton_on=pool)
                yield
                yield
                d = tt(dve, hs(o_sb), hs(o_sb), bcast_last(o_rs, HD), ALU.mult, dr)
                g_ = tt(pool, o_sb, o_sb, gate_f[s], ALU.mult, d)
                tile_read[t] = (g_, p, d)
                bi, fr = yield from misc()
                for g in range(G2):
                    p = turn(bank[bi][:, g * P:(g + 1) * P], o_sb[:, g * P:(g + 1) * P], fr, g_, signal=(g == G2 - 1))
                o_free[0] = p
                a = copy_act(oT, bank[bi][:, 0:DM], p, oT_free[0])
                release(bi, a)
                yield
                bi, fr = yield from misc()
                for k in range(KD):
                    p = mm(bank[bi][:, 0:DM], oT[:, k * P:(k + 1) * P], w_out[:, k, :], a, fr,
                           start=(k == 0), stop=(k == KD - 1), signal=(k == KD - 1))
                oT_free[0] = p
                d = tt(dve, X[:, t, :], bank[bi][:, 0:DM], X[:, t, :], ALU.add, p)
                release(bi, d)
                st_last[0] = tile_stats(t, d)
                yield

            S_end = [take(P) for _ in range(G2)]
            s_free, s_end_free, s_hold = [None] * G2, [None] * G2, {}

            def solves(slot):
                for _ in range(SLOT_LAG * slot):
                    yield
                for t in range(NT):
                    for grp in (slot, slot + 2):
                        yield from solve(t, grp, slot)

            def around():
                yield from prepare(0)
                yield from prepare(1)
                for t in range(NT):
                    while any((t, g) not in group_ready for g in range(4)):
                        yield
                    yield from scan(t)
                    if t + 2 < NT:
                        yield from prepare(t + 2)

            alternate([solves(0), forms(), solves(1), around()])
            phase()

        def state_space():
            norm_factors(st_last[0])
            U = take(NT * DM).rearrange("p (t d) -> p t d", t=NT)
            CPG = 16
            T = [take(CPG * P) for _ in range(4)]
            S = [[take(2 * DM) for _ in range(2)] for _ in range(NT // TB)]
            Z = [take(2 * DM) for _ in range(2)]
            W = [take(2 * DM) for _ in range(2)]
            N2 = [take(2 * DM) for _ in range(2)]
            t_sem = [sem(f"toeplitz_in{i}") for i in range(4)]
            t_free = [None] * 4
            n_loads = DM // CPG

            def load_toeplitz(i):
                r = i % 4
                sp.wait(t_free[r])
                src = bass.AP(tensor=taps_dram, offset=i * CPG * 2 * P + 1, ap=[[1, P], [2 * P, CPG], [1, P]])
                sp.queue.append(lambda eng: eng.dma_start(T[r].rearrange("p (h l) -> p h l", h=CPG), src).then_inc(t_sem[r], 16))
                return (t_sem[r], 16 * (i // 4 + 1))

            t_ready = {i: load_toeplitz(i) for i in range(min(4, n_loads))}
            u_ready, n_free, f_free = None, [None, None], [None, None]
            for i in range(NT // 2):
                r = i % 2
                for j in range(2):
                    d = normalize(N2[r][:, j * DM:(j + 1) * DM], 2 * i + j, n_free[r])
                p = mm(bank[6 + r][:], flip, N2[r], d, f_free[r])
                n_free[r] = p
                pair = U[:, 2 * i:2 * i + 2, :]
                f_free[r] = tt(dve, pair, bank[6 + r][:].rearrange("p (t d) -> p t d", t=2), bcast_mid(gamma_row[:], 2), ALU.mult, p)
                u_ready = tt(pool, pair, pair, bcast_mid(beta_row[:], 2), ALU.add, f_free[r])
            lam_re, lam_im = pow_re[:, P:P + 1], pow_im[:, P:P + 1]
            b_free, y_free, z_free, w_free = [None] * 2, [None] * 2, [None] * 2, [None] * 2
            n = [0]

            def between():
                for tt_ in range(TB):
                    for q in range(NT // TB):
                        t = q * TB + tt_
                        r = n[0] % 2
                        n[0] += 1
                        prev, cur = S[q][(tt_ + 1) % 2], S[q][tt_ % 2]
                        if tt_ > 0:
                            z, w = Z[r], W[r]
                            g1 = tt(pool, z[:, DM:], C_re[:], prev[:, DM:], ALU.mult, s_ready[q], z_free[r])
                            g2 = tt(pool, w[:, DM:], C_im[:], prev[:, 0:DM], ALU.mult, w_free[r])
                            g2 = tt(pool, z[:, DM:], z[:, DM:], w[:, DM:], ALU.add, g2)
                            d1 = tt(dve, z[:, 0:DM], C_re[:], prev[:, 0:DM], ALU.mult, s_ready[q], z_free[r])
                            d2 = tt(dve, w[:, 0:DM], C_im[:], prev[:, DM:], ALU.mult)
                            d2 = tt(dve, z[:, 0:DM], z[:, 0:DM], w[:, 0:DM], ALU.subtract, d2)
                            w_free[r] = g2
                            y = bank[2 + r][:, 0:DM]
                            mm(y, pow_re[:, 1:P + 1], z[:, 0:DM], d2, y_free[r], stop=False, signal=False)
                            p = mm(y, neg_pow_im[:, 1:P + 1], z[:, DM:], g2, start=False)
                            z_free[r] = p
                            y_free[r] = tt(dve, X[:, t, :], y, X[:, t, :], ALU.add, p)
                        if tt_ + 1 < TB:
                            bk = bank[r]
                            mm(bk[:, 0:DM], into_re[:], U[:, t, :], u_ready, b_free[r], signal=False)
                            p = mm(bk[:, DM:], into_im[:], U[:, t, :])
                            if tt_ == 0:
                                d = copy(cur, bk[:], p)
                            else:
                                d = stt(cur[:, 0:DM], prev[:, 0:DM], lam_re, bk[:, 0:DM], ALU.mult, ALU.add, p, g2)
                                d3 = stt(cur[:, DM:], prev[:, DM:], lam_re, bk[:, DM:], ALU.mult, ALU.add, p)
                                b_free[r] = d3
                                d = stt(cur[:, 0:DM], prev[:, DM:], step_im_neg[:], cur[:, 0:DM], ALU.mult, ALU.add, d3)
                                d = stt(cur[:, DM:], prev[:, 0:DM], lam_im, cur[:, DM:], ALU.mult, ALU.add, d)
                            if tt_ == 0:
                                b_free[r] = d
                            s_ready[q] = d
                        yield

            s_ready = [None] * (NT // TB)
            h_free = [None, None]

            def inside():
                for i in range(n_loads):
                    r, bk = i % 4, bank[4 + i % 2]
                    for c in range(CPG):
                        h = i * CPG + c
                        p = mm(bk[:, c * NT:(c + 1) * NT], T[r][:, c * P:(c + 1) * P], U[:, :, h], t_ready[i], u_ready,
                               h_free[i % 2], signal=(c == CPG - 1))
                        if c % 8 == 7:
                            yield
                    t_free[r] = p
                    if i + 4 < n_loads:
                        t_ready[i + 4] = load_toeplitz(i + 4)
                    xv = X[:, :, i * CPG:(i + 1) * CPG]
                    h_free[i % 2] = tt(dve, xv, bk[:, 0:CPG * NT].rearrange("p (c t) -> p t c", t=NT), xv, ALU.add,
                                       p, *y_free)
            alternate([between(), inside()])
            for r in range(4):
                dma_tokens.append((t_sem[r], 16 * ((n_loads - 1 - r) // 4 + 1)))
            d = (dve.sem, dve.count)
            for t in range(NT):
                st_last[0] = tile_stats(t, d)
            phase()

        st_last = [st]
        swiglu_ffn()
        delta_attention()
        swiglu_ffn()
        binary_ffn()
        state_space()
        binary_ffn(last=True)

        block = ctx.enter_context(nc.Block())
        block.tensor(pe.replay)
        block.scalar(act.replay)
        block.vector(dve.replay)
        block.gpsimd(pool.replay)
        block.sync(sp.replay)


def constants():
    import numpy as np
    i = np.arange(P)
    same = (i[:, None] // CH) == (i[None, :] // CH)
    parts = [np.eye(P), (i[:, None] <= i[None, :]) & same, (i[:, None] > i[None, :]) & same,
             (i[:, None] < i[None, :]) & same, (i[:, None] // HD) == (i[None, :] // HD),
             (i[:, None] // HD) == np.arange(8)[None, :], (i[:, None] // CH) == np.arange(2)[None, :],
             np.eye(P)[::-1]]
    return np.concatenate([np.asarray(p, np.float32) for p in parts], axis=1)


_RENAMED = {"w_gate": "L0_ffn_w_gate", "w_up": "L0_ffn_w_up", "w_down": "L0_ffn_w_down", "w_bin": "L1_ffn_weights",
            "scale": "L1_ffn_scale", "bias": "L1_ffn_bias", "gamma": "L1_attn_gamma", "beta": "L1_attn_beta",
            "lam_re": "L1_attn_Lambda_real", "lam_im": "L1_attn_Lambda_imag", "C_re": "L1_attn_C_real",
            "C_im": "L1_attn_C_imag", "param_D": "L1_attn_param_D", "Wq": "L0_attn_Wq", "Wk": "L0_attn_Wk",
            "Wv": "L0_attn_Wv", "Wg": "L0_attn_Wg", "Wo": "L0_attn_Wo", "Wb": "L0_attn_Wb", "Wa": "L0_attn_Wa",
            "dt_bias": "L0_attn_dt_bias", "A_log": "L0_attn_A_log", "norm_w": "L0_attn_norm_w"}
_TRANSPOSED = ("w_gate", "w_up", "w_down", "w_bin", "C_re", "C_im")


def kernel(**inputs):
    import numpy as np
    import concourse.bacc as bacc
    from concourse.bass_utils import run_bass_kernel_spmd as run

    nc = bacc.Bacc("TRN2", target_bir_lowering=False, num_devices=1)
    x = np.asarray(inputs["L0_attn_x"])
    B, L, D = x.shape
    arrays = {"x": np.ascontiguousarray(x.reshape(B * L, D)), "consts": constants()}
    for name, full in _RENAMED.items():
        a = np.asarray(inputs[full])
        if name == "param_D":
            a = a.reshape(KD, P).T
        arrays[name] = np.ascontiguousarray(a.T if name in _TRANSPOSED else a)
    io = {n: nc.dram_tensor(f"in_{n}", a.shape, mybir.dt.from_np(a.dtype), kind="ExternalInput").ap()
          for n, a in arrays.items()}
    io["out"] = nc.dram_tensor("out", (B * L, D), F32, kind="ExternalOutput").ap()
    build(nc, io, B * L // P, L // P)
    ins = {f"in_{n}": a for n, a in arrays.items()}
    r = run(nc, [ins], core_ids=[0])
    return r.results[0]["out"].reshape(B, L, D)
```
